# Optimizing a Trainium2 kernel written in Bass

```python
import numpy as np
import jax
import jax.numpy as jnp

def _softmax(x, axis=-1):
    return jax.nn.softmax(x, axis=axis)

def _gelu(x):
    return jax.nn.gelu(x, approximate=True)

def _silu(x):
    return jax.nn.silu(x)

def _sigmoid(x):
    return jax.nn.sigmoid(x)

def _layernorm(x, axis=-1, eps=1e-05):
    m = jnp.mean(x, axis=axis, keepdims=True)
    v = jnp.var(x, axis=axis, keepdims=True)
    return (x - m) / jnp.sqrt(v + eps)

def _scatter_add(tgt, idx, src, axis=0):
    return tgt.at[idx].add(src)

def _segment_sum(src, seg, n):
    return jax.ops.segment_sum(src, seg, n)
kernel_name = 'mk_rec_standalone_d1_rec_r8_78d53a'

def setup_inputs(seed: int=0):
    np.random.seed(seed)
    _w = jnp.asarray

    def _rec_inputs():
        import jax
        import jax.numpy as jnp
        _rk = jax.random.key(seed)
        r_x = -0.000520686 + 1.00062 * jax.random.normal(jax.random.fold_in(_rk, 1), (2048, 512), jnp.float32)
        return r_x
    r_x = _rec_inputs()

    def _L0_rec_setup():
        import jax, jax.numpy as jnp
        import numpy as np
        B, N, H, L = (512, 512, 1024, 8)
        key = jax.random.key(seed)
        k1, k2, k3, k4 = jax.random.split(key, 4)
        x = jax.random.normal(k1, (B, N), dtype=jnp.float32)
        beta = jax.random.uniform(k2, (H, L, N), dtype=jnp.float32)
        bound = 1.0 / np.sqrt(N)
        W = jax.random.uniform(k3, (H, N), minval=-bound, maxval=bound, dtype=jnp.float32)
        b = jax.random.uniform(k4, (H,), minval=-bound, maxval=bound, dtype=jnp.float32)
        return {'x': x, 'beta': beta, 'W': W, 'b': b}
    _L0_rec_all = _L0_rec_setup()
    _L0_rec_in = {k: v for k, v in _L0_rec_all.items() if k in ('beta', 'W', 'b')}
    del _L0_rec_all
    return {'r_x': r_x, 'L0_rec_beta': _L0_rec_in['beta'], 'L0_rec_W': _L0_rec_in['W'], 'L0_rec_b': _L0_rec_in['b']}

def reference(r_x, L0_rec_beta, L0_rec_W, L0_rec_b):
    import jax
    import jax.numpy as jnp

    def _L0_rec_ref(x, beta, W, b):
        import jax, jax.numpy as jnp
        import numpy as np
        B, N, H, L = (512, 512, 1024, 8)
        s = jnp.einsum('bn,hln->bhl', x, beta)
        ssq = jnp.einsum('bn,hln->bhl', x * x, beta * beta)
        fm = 0.5 * jnp.sum(s * s - ssq, axis=-1)
        linear_out = x @ W.T + b
        return fm + linear_out
    y = _L0_rec_ref(r_x, L0_rec_beta, L0_rec_W, L0_rec_b)
    return y

_drawn_inputs = setup_inputs


def setup_inputs(seed=0):
    import zlib

    import numpy as np

    out = dict(_drawn_inputs(seed))
    spreads = {}
    factors = {'L0_rec_W': 64.0, 'L0_rec_b': 64.0}
    for name, (base, spread) in spreads.items():
        noise = np.random.default_rng([zlib.crc32(name.encode()), seed]).standard_normal(out[name].shape)
        drawn = base * np.exp(spread * noise) if base else spread * noise
        out[name] = jnp.asarray(drawn.astype(out[name].dtype))
    for name, factor in factors.items():
        out[name] = (out[name] * factor).astype(out[name].dtype)
    return out
```

```python
from contextlib import ExitStack

import concourse.bass as bass
from concourse import mybir

P = 128
B, N, H, L = 2048, 512, 1024, 8
K_TILES = N // P
TILES = B // P
COLS = 512
CHUNK_H = COLS // L
CHUNKS = H // CHUNK_H
HALVES = H // COLS
HALF_CHUNKS = CHUNKS // HALVES
BANKS = 8
SQ_SLOTS = 4
GROUP = 8
GROUPS = TILES // GROUP
PREP = K_TILES // GROUPS


def fm_layer(nc, x_t, beta_t, w_t, bias, out):
    f32 = mybir.dt.float32
    f32r = mybir.dt.float32r
    ALU = mybir.AluOpType
    ACT = mybir.ActivationFunctionType
    AX_X = mybir.AxisListType.X

    with ExitStack() as ctx:
        def sb(name, shape, dt=f32):
            return ctx.enter_context(nc.sbuf_tensor(name, shape, dt))

        def sem(name):
            return ctx.enter_context(nc.semaphore(name))

        x_hi = sb("x_hi", [P, TILES, N], f32r)
        x_lo = sb("x_lo", [P, TILES, N], f32r)
        acc = sb("acc", [P, TILES, COLS])
        beta_raw = sb("beta_raw", [P, K_TILES, COLS])
        beta_hi = sb("beta_hi", [P, 2, K_TILES, COLS], f32r)
        beta_lo = sb("beta_lo", [P, 2, K_TILES, COLS], f32r)
        beta_sq = sb("beta_sq", [P, COLS])
        q = sb("q", [P, K_TILES, COLS])
        q_hi = sb("q_hi", [P, K_TILES, COLS], f32r)
        q_lo = sb("q_lo", [P, K_TILES, COLS], f32r)
        w_raw = sb("w_raw", [P, 2, COLS])
        w_hi = sb("w_hi", [P, K_TILES, COLS], f32r)
        w_lo = sb("w_lo", [P, K_TILES, COLS], f32r)
        x_whole = sb("x_whole", [P, N])
        x_sq = sb("x_sq", [P, N])
        x_sq_hi = sb("x_sq_hi", [P, 2, N], f32r)
        x_sq_lo = sb("x_sq_lo", [P, 2, N], f32r)
        squares = sb("squares", [P, SQ_SLOTS, COLS])
        bias_all = sb("bias_all", [P, H])
        banks = [ctx.enter_context(nc.psum_tensor(f"bank{i}", [P, COLS], f32)) for i in range(BANKS)]

        beta_loaded = [sem(f"beta_loaded{k}") for k in range(K_TILES)]
        x_loaded = [sem(f"x_loaded{t}") for t in range(TILES)]
        w_loaded = [sem(f"w_loaded{i}") for i in range(2)]
        bias_loaded = sem("bias_loaded")
        stored = sem("stored")
        x_hi_ready = sem("x_hi_ready")
        x_lo_ready = sem("x_lo_ready")
        beta_hi_ready = sem("beta_hi_ready")
        beta_lo_ready = sem("beta_lo_ready")
        beta_squared = sem("beta_squared")
        q_summed = sem("q_summed")
        w_hi_ready = sem("w_hi_ready")
        w_lo_ready = sem("w_lo_ready")
        q_hi_ready = sem("q_hi_ready")
        q_lo_ready = sem("q_lo_ready")
        x_whole_ready = sem("x_whole_ready")
        x_sq_ready = sem("x_sq_ready")
        x_sq_hi_ready = sem("x_sq_hi_ready")
        x_sq_lo_ready = sem("x_sq_lo_ready")
        dots_made = sem("dots_made")
        dots_squared = sem("dots_squared")
        dots_summed = sem("dots_summed")
        linear_made = sem("linear_made")
        sums_scaled = sem("sums_scaled")
        linear_added = sem("linear_added")

        block = ctx.enter_context(nc.Block())

        def cols(i):
            return slice(i * P, (i + 1) * P)

        @block.sync
        def _(sp):
            sp.dma_start(beta_raw[:, 0, :], beta_t[0]).then_inc(beta_loaded[0], 16)
            sp.dma_start(acc[:, 0, :], x_t[0]).then_inc(x_loaded[0], 16)
            for k in range(1, K_TILES):
                sp.dma_start(beta_raw[:, k, :], beta_t[k]).then_inc(beta_loaded[k], 16)
            for t in range(1, TILES):
                sp.dma_start(acc[:, t, :], x_t[t]).then_inc(x_loaded[t], 16)
            sp.dma_start(bias_all[:, :], bias.to_broadcast([P, H])).then_inc(bias_loaded, 16)
            loaded = 1
            for half in range(HALVES):
                until = min((half + 1) * HALF_CHUNKS + 2, CHUNKS)
                with sp.Fori(loaded, until) as chunk:
                    for k in range(K_TILES):
                        sp.wait_ge(beta_squared, (chunk - 1) * K_TILES + k + 1)
                        sp.dma_start(beta_raw[:, k, :],
                                     beta_t[bass.ds(chunk * K_TILES + k, 1)].rearrange("a p c -> (a p) c")
                                     ).then_inc(beta_loaded[k], 16)
                loaded = until
                with sp.Fori(0, TILES) as t:
                    sp.wait_ge(linear_added, BANKS + half * TILES + 1 + t)
                    sp.dma_start(out[bass.ds(t * P, P), half * COLS:(half + 1) * COLS],
                                 acc[:, t, :]).then_inc(stored, 16)
            sp.wait_ge(stored, 16 * HALVES * TILES)

        @block.gpsimd
        def _(pool):
            for piece in range(HALVES * K_TILES):
                if piece >= 2:
                    pool.wait_ge(w_lo_ready, piece - 1)
                pool.dma_start(w_raw[:, piece % 2, :], w_t[piece]).then_inc(w_loaded[piece % 2], 16)

        @block.tensor
        def _(pe):
            def passes(bank, a_hi, a_lo, b_hi, b_lo, start, stop):
                nc.tensor.matmul(bank, a_hi, b_hi, start=start, stop=False)
                nc.tensor.matmul(bank, a_hi, b_lo, start=False, stop=False)
                return nc.tensor.matmul(bank, a_lo, b_hi, start=False, stop=stop)


            def linear_tile(half, t):
                n = half * TILES + t
                if t < BANKS:
                    pe.wait_ge(dots_squared, (half + 1) * HALF_CHUNKS * TILES + t + 1)
                else:
                    pe.wait_ge(linear_added, n + 1)
                for k in range(K_TILES):
                    if t == 0:
                        pe.wait_ge(w_lo_ready, half * K_TILES + k + 1)
                    passes(banks[t % BANKS][:, :], x_hi[:, t, cols(k)], x_lo[:, t, cols(k)],
                           w_hi[:, k, :], w_lo[:, k, :], k == 0, False)
                pe.wait_ge(x_sq_lo_ready, n + 1)
                for k in range(K_TILES):
                    if t == 0:
                        pe.wait_ge(q_lo_ready, half * K_TILES + k + 1)
                    last = passes(banks[t % BANKS][:, :], x_sq_hi[:, t % 2, cols(k)],
                                  x_sq_lo[:, t % 2, cols(k)],
                                  q_hi[:, k, :], q_lo[:, k, :], False, k == K_TILES - 1)
                last.then_inc(linear_made, 1)

            with pe.Fori(0, HALVES) as half:
                with pe.Fori(0, HALF_CHUNKS // 2) as pair:
                    for slot in range(2):
                        for t in range(TILES):
                            n = (half * HALF_CHUNKS + pair * 2 + slot) * TILES + t
                            pe.wait_ge(x_lo_ready, t + 1)
                            pe.wait_ge(dots_squared, n + 1)
                            if t < BANKS:
                                pe.wait_ge(linear_added, half * TILES + t + 1)
                            for k in range(K_TILES):
                                if t == 0:
                                    pe.wait_ge(beta_lo_ready,
                                               (half * HALF_CHUNKS + pair * 2 + slot) * K_TILES + k + 1)
                                last = passes(banks[t % BANKS][:, :], x_hi[:, t, cols(k)],
                                              x_lo[:, t, cols(k)], beta_hi[:, slot, k, :],
                                              beta_lo[:, slot, k, :], k == 0, k == K_TILES - 1)
                            last.then_inc(dots_made, 1)
                for t in range(TILES):
                    linear_tile(half, t)

        @block.scalar
        def _(act):
            act.sem_inc(dots_squared, BANKS)

            def beta_high(chunk, slot, k):
                act.wait_ge(beta_loaded[k], 16 * (chunk + 1))
                nc.scalar.copy(beta_hi[:, slot, k, :], beta_raw[:, k, :]).then_inc(beta_hi_ready, 1)

            def x_high(t):
                act.wait_ge(x_loaded[t], 16)
                nc.scalar.copy(x_hi[:, t, :], acc[:, t, :]).then_inc(x_hi_ready, 1)

            def chunk_steps(chunk, prepare):
                slot = prepare
                for group in range(GROUPS):
                    for j in range(GROUP):
                        t = group * GROUP + j
                        n = chunk * TILES + t
                        act.wait_ge(dots_made, n + 1)
                        act.wait_ge(dots_summed, n + 1)
                        nc.scalar.activation(squares[:, t % SQ_SLOTS, :], banks[t % BANKS][:, :],
                                             ACT.Square).then_inc(dots_squared, 1)
                        if slot is not None and j % (GROUP // PREP) == 0:
                            beta_high(chunk + 1, slot, group * PREP + j // (GROUP // PREP))

            beta_high(0, 0, 0)
            x_high(0)
            for k in range(1, K_TILES):
                beta_high(0, 0, k)
            for t in range(1, TILES):
                x_high(t)
            for half in range(HALVES):
                first = half * HALF_CHUNKS
                with act.Fori(0, HALF_CHUNKS // 2 - 1) as pair:
                    chunk_steps(first + pair * 2, 1)
                    chunk_steps(first + pair * 2 + 1, 0)
                chunk_steps(first + HALF_CHUNKS - 2, 1)
                if half:
                    act.wait_ge(linear_made, half * TILES)
                for k in range(K_TILES):
                    piece = half * K_TILES + k
                    act.wait_ge(w_loaded[piece % 2], 16 * (piece // 2 + 1))
                    nc.scalar.copy(w_hi[:, k, :], w_raw[:, piece % 2, :]).then_inc(w_hi_ready, 1)
                act.wait_ge(q_summed, (first + HALF_CHUNKS) * K_TILES)
                for k in range(K_TILES):
                    nc.scalar.mul(q_hi[:, k, :], q[:, k, :], -0.5).then_inc(q_hi_ready, 1)
                chunk_steps(first + HALF_CHUNKS - 1, 0 if half < HALVES - 1 else None)
                for t in range(TILES):
                    n = half * TILES + t
                    act.wait_ge(x_sq_ready, n + 1)
                    if n >= 2:
                        act.wait_ge(linear_made, n - 1)
                    nc.scalar.copy(x_sq_hi[:, t % 2, :], x_sq[:, :]).then_inc(x_sq_hi_ready, 1)

        @block.vector
        def _(dve):
            dve.sem_inc(linear_added, BANKS)
            dve.sem_inc(dots_summed, SQ_SLOTS)

            def as_f32(ap):
                return ap.bitcast(f32)

            def beta_low(chunk, slot, k):
                dve.wait_ge(beta_hi_ready, chunk * K_TILES + k + 1)
                nc.vector.tensor_tensor(beta_lo[:, slot, k, :], beta_raw[:, k, :],
                                        as_f32(beta_hi[:, slot, k, :]), ALU.subtract
                                        ).then_inc(beta_lo_ready, 1)

            def beta_to_q(chunk, at, k):
                n = chunk * K_TILES + k
                if not isinstance(n, int) or n:
                    dve.wait_ge(q_summed, n)
                nc.vector.tensor_tensor(beta_sq[:, :], beta_raw[:, k, :], beta_raw[:, k, :],
                                        ALU.mult).then_inc(beta_squared, 1)
                dve.wait_ge(beta_squared, n + 1)
                nc.vector.tensor_reduce(q[:, k, bass.ds(at * CHUNK_H, CHUNK_H)],
                                        beta_sq[:, :].rearrange("p (h l) -> p h l", l=L),
                                        AX_X, ALU.add).then_inc(q_summed, 1)

            def x_low(t):
                dve.wait_ge(x_hi_ready, t + 1)
                nc.vector.tensor_tensor(x_lo[:, t, :], acc[:, t, :], as_f32(x_hi[:, t, :]),
                                        ALU.subtract).then_inc(x_lo_ready, 1)

            def chunk_steps(first, at, prepare, prepare_at):
                chunk = first + at
                for group in range(GROUPS):
                    for j in range(GROUP):
                        t = group * GROUP + j
                        dve.wait_ge(dots_squared, BANKS + chunk * TILES + t + 1)
                        nc.vector.tensor_reduce(
                            acc[:, t, bass.ds(at * CHUNK_H, CHUNK_H)],
                            squares[:, t % SQ_SLOTS, :].rearrange("p (h l) -> p h l", l=L),
                            AX_X, ALU.add).then_inc(dots_summed, 1)
                        if prepare is not None and j % (GROUP // PREP) == 0:
                            k = group * PREP + j // (GROUP // PREP)
                            beta_low(chunk + 1, prepare, k)
                            beta_to_q(chunk + 1, prepare_at, k)

            def square_x(half, t):
                n = half * TILES + t
                if n:
                    dve.wait_ge(x_sq_lo_ready, n)
                nc.vector.tensor_tensor(x_whole[:, :], as_f32(x_hi[:, t, :]), as_f32(x_lo[:, t, :]),
                                        ALU.add).then_inc(x_whole_ready, 1)
                dve.wait_ge(x_whole_ready, n + 1)
                nc.vector.tensor_tensor(x_sq[:, :], x_whole[:, :], x_whole[:, :],
                                        ALU.mult).then_inc(x_sq_ready, 1)
                dve.wait_ge(x_sq_ready, n + 1)
                dve.wait_ge(x_sq_hi_ready, n + 1)
                nc.vector.tensor_tensor(x_sq_lo[:, t % 2, :], x_sq[:, :], as_f32(x_sq_hi[:, t % 2, :]),
                                        ALU.subtract).then_inc(x_sq_lo_ready, 1)

            beta_low(0, 0, 0)
            x_low(0)
            for k in range(1, K_TILES):
                beta_low(0, 0, k)
            for t in range(1, TILES):
                x_low(t)
            dve.wait_ge(x_lo_ready, TILES)
            for k in range(K_TILES):
                beta_to_q(0, 0, k)
            for half in range(HALVES):
                first = half * HALF_CHUNKS
                if half:
                    dve.wait_ge(stored, 16 * half * TILES)
                with dve.Fori(0, HALF_CHUNKS // 2 - 1) as pair:
                    chunk_steps(first, pair * 2, 1, pair * 2 + 1)
                    chunk_steps(first, pair * 2 + 1, 0, pair * 2 + 2)
                chunk_steps(first, HALF_CHUNKS - 2, 1, HALF_CHUNKS - 1)
                for k in range(K_TILES):
                    piece = half * K_TILES + k
                    dve.wait_ge(w_hi_ready, piece + 1)
                    nc.vector.tensor_tensor(w_lo[:, k, :], w_raw[:, piece % 2, :], as_f32(w_hi[:, k, :]),
                                            ALU.subtract).then_inc(w_lo_ready, 1)
                dve.wait_ge(q_summed, (first + HALF_CHUNKS) * K_TILES)
                for k in range(K_TILES):
                    dve.wait_ge(q_hi_ready, half * K_TILES + k + 1)
                    nc.vector.scalar_tensor_tensor(q_lo[:, k, :], q[:, k, :], -0.5, as_f32(q_hi[:, k, :]),
                                                   ALU.mult, ALU.subtract).then_inc(q_lo_ready, 1)
                dve.wait_ge(q_lo_ready, (half + 1) * K_TILES)
                chunk_steps(first, HALF_CHUNKS - 1, 0 if half < HALVES - 1 else None, 0)
                if half == 0:
                    dve.wait_ge(bias_loaded, 16)
                dve.wait_ge(dots_summed, SQ_SLOTS + (first + HALF_CHUNKS) * TILES)
                square_x(half, 0)
                for t in range(TILES):
                    n = half * TILES + t
                    nc.vector.scalar_tensor_tensor(acc[:, t, :], acc[:, t, :], 0.5,
                                                   bias_all[:, half * COLS:(half + 1) * COLS],
                                                   ALU.mult, ALU.add).then_inc(sums_scaled, 1)
                    if t + 1 < TILES:
                        square_x(half, t + 1)
                    dve.wait_ge(sums_scaled, n + 1)
                    dve.wait_ge(linear_made, n + 1)
                    nc.vector.tensor_tensor(acc[:, t, :], acc[:, t, :], banks[t % BANKS][:, :],
                                            ALU.add).then_inc(linear_added, 1)


def kernel(r_x, L0_rec_beta, L0_rec_W, L0_rec_b):
    import numpy as np
    import concourse.bacc as bacc
    from concourse.bass_utils import run_bass_kernel_spmd

    x, beta, w, b = (np.asarray(a) for a in (r_x, L0_rec_beta, L0_rec_W, L0_rec_b))
    arrays = {
        "x_t": x.reshape(TILES, P, K_TILES, P).transpose(0, 3, 2, 1).reshape(TILES, P, N),
        "beta_t": beta.reshape(CHUNKS, CHUNK_H, L, K_TILES, P).transpose(0, 3, 4, 1, 2)
                      .reshape(CHUNKS * K_TILES, P, COLS),
        "w_t": w.reshape(HALVES, COLS, K_TILES, P).transpose(0, 2, 3, 1).reshape(HALVES * K_TILES, P, COLS),
        "bias": b.reshape(1, H),
    }
    arrays = {name: np.ascontiguousarray(a) for name, a in arrays.items()}
    nc = bacc.Bacc("TRN2", target_bir_lowering=False, num_devices=1)
    args = [nc.dram_tensor(name, a.shape, mybir.dt.from_np(a.dtype), kind="ExternalInput").ap()
            for name, a in arrays.items()]
    out = nc.dram_tensor("out", (B, H), mybir.dt.float32, kind="ExternalOutput").ap()
    fm_layer(nc, *args, out)
    result = run_bass_kernel_spmd(nc, [arrays], core_ids=[0])
    return result.results[0]["out"]
```
